# Optimizing a Trainium2 kernel written in Bass

```python
import numpy as np
import jax
import jax.numpy as jnp

def _softmax(x, axis=-1):
    return jax.nn.softmax(x, axis=axis)

def _gelu(x):
    return jax.nn.gelu(x, approximate=True)

def _silu(x):
    return jax.nn.silu(x)

def _sigmoid(x):
    return jax.nn.sigmoid(x)

def _layernorm(x, axis=-1, eps=1e-05):
    m = jnp.mean(x, axis=axis, keepdims=True)
    v = jnp.var(x, axis=axis, keepdims=True)
    return (x - m) / jnp.sqrt(v + eps)

def _scatter_add(tgt, idx, src, axis=0):
    return tgt.at[idx].add(src)

def _segment_sum(src, seg, n):
    return jax.ops.segment_sum(src, seg, n)
kernel_name = 'mk_cond_resid_d1_seqx_r4_102d6b'

def setup_inputs(seed: int=0):
    np.random.seed(seed)
    _w = jnp.asarray

    def _rec_inputs():
        import jax
        import jax.numpy as jnp
        _rk = jax.random.key(seed)
        x = -7.109e-05 + 0.9999 * jax.random.normal(jax.random.fold_in(_rk, 1), (64, 64, 512), jnp.float32)
        _lenS = 64 - jax.random.randint(jax.random.fold_in(_rk, 7), (64,), 0, max(1, 64 // 4) + 1, jnp.int32)
        _lenS2 = 64 - jax.random.randint(jax.random.fold_in(_rk, 8), (64,), 0, max(1, 64 // 4) + 1, jnp.int32)
        itok_B_1_198 = jax.random.randint(jax.random.fold_in(_rk, 11), (64,), 1, 199, jnp.int32)
        return (x, itok_B_1_198)
    x, itok_B_1_198 = _rec_inputs()

    def _L0_cond_setup():
        import jax, jax.numpy as jnp
        import numpy as np
        B, C, T = (128, 64, 512)
        S, D = (200, 64)
        key = jax.random.key(seed)
        k1, k2, k3 = jax.random.split(key, 3)
        x = jax.random.normal(k1, (B, C, T), dtype=jnp.float32)
        conditions = jax.random.randint(k2, (B,), 0, S, dtype=jnp.int64)
        weights = jax.random.normal(k3, (S, C, D), dtype=jnp.float32) / jnp.sqrt(jnp.float32(C))
        return {'x': x, 'conditions': conditions, 'weights': weights}
    _L0_cond_all = _L0_cond_setup()
    _L0_cond_in = {k: v for k, v in _L0_cond_all.items() if k in ('weights',)}
    del _L0_cond_all
    return {'x': x, 'itok_B_1_198': itok_B_1_198, 'L0_cond_weights': _L0_cond_in['weights']}

def reference(x, itok_B_1_198, L0_cond_weights):
    import jax
    import jax.numpy as jnp

    def _L0_cond_ref(x, conditions, weights):
        import jax, jax.numpy as jnp
        import numpy as np
        B, C, T = (128, 64, 512)
        S, D = (200, 64)
        w = weights[conditions]
        return jnp.einsum('bct,bcd->bdt', x, w)
    x = x + _L0_cond_ref(x, itok_B_1_198, L0_cond_weights)
    return x

_drawn_inputs = setup_inputs


def setup_inputs(seed=0):
    import zlib

    import numpy as np

    out = dict(_drawn_inputs(seed))
    spreads = {}
    factors = {}
    for name, (base, spread) in spreads.items():
        noise = np.random.default_rng([zlib.crc32(name.encode()), seed]).standard_normal(out[name].shape)
        drawn = base * np.exp(spread * noise) if base else spread * noise
        out[name] = jnp.asarray(drawn.astype(out[name].dtype))
    for name, factor in factors.items():
        out[name] = (out[name] * factor).astype(out[name].dtype)
    return out
```

```python
import concourse.bass as bass
from concourse import mybir
from contextlib import ExitStack


def conditioned_residual_kernel(nc: bass.Bass, x: bass.AP, conditions: bass.AP, weights: bass.AP, out: bass.AP):
    fp32 = mybir.dt.float32
    i32 = mybir.dt.int32
    ALU = mybir.AluOpType

    B, C, T = x.shape
    S, _, D = weights.shape
    PAIR = 2
    P = PAIR * C
    PAIRS = B // PAIR
    U = 8
    TURNS = PAIRS // U
    CH = 2
    NCH = U // CH

    x_rows = x.rearrange("(n two) c t -> (two c) n t", two=PAIR)
    out_rows = out.rearrange("(n two) c t -> (two c) n t", two=PAIR)

    ctx = ExitStack()
    with ctx:
        x_sb = ctx.enter_context(nc.sbuf_tensor("x_sb", [P, PAIRS, T], fp32))
        w_diag = ctx.enter_context(nc.sbuf_tensor("w_diag", [P, U, PAIR * D], fp32))
        product = [ctx.enter_context(nc.psum_tensor(f"product{s}", [P, T], fp32)) for s in range(U)]

        x_loaded = [ctx.enter_context(nc.semaphore(f"x_loaded{j}")) for j in range(NCH)]
        w_loaded = [ctx.enter_context(nc.semaphore(f"w_loaded{s}")) for s in range(U)]
        w_zeroed = ctx.enter_context(nc.semaphore("w_zeroed"))
        multiplied = ctx.enter_context(nc.semaphore("multiplied"))
        added = ctx.enter_context(nc.semaphore("added"))
        stored = ctx.enter_context(nc.semaphore("stored"))
        block = ctx.enter_context(nc.Block())

        @block.sync
        def _(sp):
            def load(turn, j):
                at = turn * U + j * CH
                sp.dma_start(x_sb[:, bass.ds(at, CH), :], x_rows[:, bass.ds(at, CH), :]).then_inc(x_loaded[j], 16)

            def store(turn, j):
                at = turn * U + j * CH
                sp.wait_ge(added, at + CH)
                sp.dma_start(out_rows[:, bass.ds(at, CH), :], x_sb[:, bass.ds(at, CH), :]).then_inc(stored, 16)

            for j in range(NCH):
                load(0, j)
            with sp.Fori(0, TURNS - 1) as turn:
                for j in range(NCH):
                    sp.wait_ge(x_loaded[j], turn * 16 + 16)
                    load(turn + 1, j)
                for j in range(NCH):
                    store(turn, j)
            for j in range(NCH):
                store(TURNS - 1, j)
            sp.wait_ge(stored, 16 * TURNS * NCH)

        @block.scalar
        def _(act):
            def gather(turn, done):
                _, rows = nc.values_load_multi_w_load_instructions(
                    conditions[:, bass.ds(turn * U * PAIR, U * PAIR)], engines=[mybir.EngineType.Activation],
                    min_val=0, max_val=S - 1, skip_runtime_bounds_check_because="an index of the table")
                for s in range(U):
                    if done is not None:
                        act.wait_ge(multiplied, done * U + (s + 1))
                    for h in range(PAIR):
                        act.dma_start(w_diag[h * C:(h + 1) * C, s, h * D:(h + 1) * D],
                                      weights[bass.ds(rows[s * PAIR + h], 1), :, :].rearrange("s c d -> (s c) d")
                                      ).then_inc(w_loaded[s], 16)

            gather(0, None)
            with act.Fori(0, TURNS - 1) as done:
                gather(done + 1, done)

        @block.gpsimd
        def _(pool):
            nc.gpsimd.memset(w_diag[C:P, :, 0:D], 0.0).then_inc(w_zeroed, 1)

        @block.tensor
        def _(pe):
            def multiply(turn, s, done):
                if s % CH == 0:
                    pe.wait_ge(x_loaded[s // CH], turn * 16 + 16)
                pe.wait_ge(w_loaded[s], turn * (16 * PAIR) + 16 * PAIR)
                if done is not None:
                    pe.wait_ge(added, done * U + (s + 1))
                nc.tensor.matmul(product[s][:, :], w_diag[:, s, :], x_sb[:, bass.ds(turn * U + s, 1), :],
                                 start=True, stop=True).then_inc(multiplied, 1)

            pe.wait_ge(w_zeroed, 2)
            for s in range(U):
                multiply(0, s, None)
            with pe.Fori(0, TURNS - 1) as done:
                for s in range(U):
                    multiply(done + 1, s, done)

        @block.vector
        def _(dve):
            nc.vector.memset(w_diag[0:C, :, D:PAIR * D], 0.0).then_inc(w_zeroed, 1)
            with dve.Fori(0, TURNS) as turn:
                for s in range(U):
                    dve.wait_ge(multiplied, turn * U + (s + 1))
                    xs = x_sb[:, bass.ds(turn * U + s, 1), :]
                    nc.vector.tensor_tensor(xs, product[s][:, :].unsqueeze(1), xs, ALU.add).then_inc(added, 1)


def kernel(x, itok_B_1_198, L0_cond_weights):
    import numpy as np
    import concourse.bacc as bacc
    from concourse.bass_utils import run_bass_kernel_spmd

    nc = bacc.Bacc("TRN2", target_bir_lowering=False, num_devices=1)
    arrays = {"x": np.ascontiguousarray(x),
              "conditions": np.ascontiguousarray(itok_B_1_198).reshape(1, -1),
              "weights": np.ascontiguousarray(L0_cond_weights)}
    args = [nc.dram_tensor(name, a.shape, mybir.dt.from_np(a.dtype), kind="ExternalInput").ap()
            for name, a in arrays.items()]
    out = nc.dram_tensor("out", x.shape, mybir.dt.float32, kind="ExternalOutput").ap()
    conditioned_residual_kernel(nc, *args, out)
    result = run_bass_kernel_spmd(nc, [arrays], core_ids=[0])
    return result.results[0]["out"]
```

```python
import concourse.bass as bass
from concourse import mybir
from contextlib import ExitStack


def conditioned_residual_kernel(nc: bass.Bass, x: bass.AP, conditions: bass.AP, weights: bass.AP, out: bass.AP):
    fp32 = mybir.dt.float32
    i32 = mybir.dt.int32
    ALU = mybir.AluOpType

    B, C, T = x.shape
    S, _, D = weights.shape
    PAIR = 2
    P = PAIR * C
    PAIRS = B // PAIR
    Q = 32
    K = C // Q
    U = 8
    TURNS = PAIRS // U
    CH = 2
    NCH = U // CH
    WG = 4
    NWG = U // WG
    WARM = 8

    x_rows = x.rearrange("(n two) c t -> (two c) n t", two=PAIR)
    out_rows = out.rearrange("(n two) c t -> (two c) n t", two=PAIR)
    condition_of = conditions.rearrange("(n two) one -> two n one", two=PAIR)
    table = weights.rearrange("s (k c) d -> (s k) (c d)", k=K)

    ctx = ExitStack()
    with ctx:
        def sbuf(name, shape, dtype):
            return ctx.enter_context(nc.sbuf_tensor(name, shape, dtype))

        def semaphore(name):
            return ctx.enter_context(nc.semaphore(name))

        x_sb = sbuf("x_sb", [P, PAIRS, T], fp32)
        condition = sbuf("condition", [P, 1], i32)
        piece = sbuf("piece", [P, 1], fp32)
        table_row = sbuf("table_row", [P, 1], i32)
        gathered = sbuf("gathered", [P, Q * D], fp32)
        w_all = sbuf("w_all", [P, D, PAIRS], fp32)
        zeros = sbuf("zeros", [P, T], mybir.dt.bfloat16)
        w_diag = sbuf("w_diag", [P, U, PAIR * D], fp32)
        product = [ctx.enter_context(nc.psum_tensor(f"product{s}", [P, T], fp32)) for s in range(U)]

        x_loaded = [semaphore(f"x_loaded{j}") for j in range(NCH)]
        zeros_set = semaphore("zeros_set")
        condition_loaded = semaphore("condition_loaded")
        pieces_set = semaphore("pieces_set")
        rows_known = semaphore("rows_known")
        gather_started = semaphore("gather_started")
        w_gathered = semaphore("w_gathered")
        w_transposed = semaphore("w_transposed")
        w_zeroed = semaphore("w_zeroed")
        w_placed = semaphore("w_placed")
        multiplied = semaphore("multiplied")
        added = semaphore("added")
        stored = semaphore("stored")
        block = ctx.enter_context(nc.Block())

        @block.sync
        def _(sp):
            def load(turn, j):
                at = turn * U + j * CH
                sp.dma_start(x_sb[:, bass.ds(at, CH), :], x_rows[:, bass.ds(at, CH), :]).then_inc(x_loaded[j], 16)

            for j in range(NCH):
                load(0, j)
            sp.wait_ge(gather_started, 1)
            with sp.Fori(0, TURNS - 1) as before:
                for j in range(NCH):
                    sp.wait_ge(x_loaded[j], before * 16 + 16)
                    load(before + 1, j)

        @block.scalar
        def _(act):
            def place(turn, g, done):
                if done is not None:
                    act.wait_ge(multiplied, done * U + (g + 1) * WG)
                for h in range(PAIR):
                    rows = slice(h * C, (h + 1) * C)
                    nc.scalar.copy(w_diag[rows, g * WG:(g + 1) * WG, h * D:(h + 1) * D],
                                   w_all[rows, :, bass.ds(turn * U + g * WG, WG)].rearrange("p d n -> p n d")
                                   ).then_inc(w_placed, 1)

            def store(turn, s, n):
                at = turn * U + s
                act.wait_ge(added, at + n)
                act.dma_start(out_rows[:, bass.ds(at, n), :], x_sb[:, bass.ds(at, n), :]).then_inc(stored, 16)

            for h in range(PAIR):
                act.dma_start(condition[h * C:(h + 1) * C, :],
                              condition_of[h:h + 1, :, :].to_broadcast([K, PAIRS, 1]),
                              allow_slow_non_contiguous=True).then_inc(condition_loaded, 16)
            act.wait_ge(w_transposed, 1)
            for g in range(NWG):
                place(0, g, None)
            with act.Fori(0, TURNS - 1) as turn:
                for g in range(NWG):
                    place(turn + 1, g, turn)
                    for s in range(g * WG, (g + 1) * WG, CH):
                        store(turn, s, CH)
            for s in range(0, U - CH, CH):
                store(TURNS - 1, s, CH)
            for s in range(U - CH, U):
                store(TURNS - 1, s, 1)
            act.wait_ge(stored, 16 * ((TURNS * U - CH) // CH + CH))

        @block.gpsimd
        def _(pool):
            nc.gpsimd.memset(w_diag[C:P, :, 0:D], 0.0).then_inc(w_zeroed, 1)
            pool.wait_ge(rows_known, 1)
            nc.gpsimd.indirect_dma_start(gathered[:, :], None, table,
                                         bass.IndirectOffsetOnAxis(ap=table_row[:, 0:1], axis=0),
                                         engine_sem=gather_started).then_inc(w_gathered, 16)

        @block.tensor
        def _(pe):
            def multiply(turn, s, done):
                if s % CH == 0:
                    pe.wait_ge(x_loaded[s // CH], turn * 16 + 16)
                if s % WG == 0:
                    pe.wait_ge(w_placed, turn * (NWG * PAIR) + (s // WG + 1) * PAIR)
                if done is not None:
                    pe.wait_ge(added, done * U + (s + 1))
                nc.tensor.matmul(product[s][:, :], w_diag[:, s, :], x_sb[:, bass.ds(turn * U + s, 1), :],
                                 start=True, stop=True).then_inc(multiplied, 1)

            pe.wait_ge(zeros_set, 1)
            pe.wait_ge(w_gathered, 16)
            for _ in range(WARM):
                nc.tensor.matmul(product[U - 1][:, :], zeros[:, 0:P], zeros[:, :], start=True, stop=True)
            pe.wait_ge(w_zeroed, 2)
            for s in range(U):
                multiply(0, s, None)
            with pe.Fori(0, TURNS - 1) as done:
                for s in range(U):
                    multiply(done + 1, s, done)

        @block.vector
        def _(dve):
            nc.vector.memset(zeros[:, :], 0.0).then_inc(zeros_set, 1)
            for q in range(P // Q):
                nc.vector.memset(piece[q * Q:(q + 1) * Q, :], float(q % K)).then_inc(pieces_set, 1)
            nc.vector.memset(w_diag[0:C, :, D:PAIR * D], 0.0).then_inc(w_zeroed, 1)
            dve.wait_ge(pieces_set, P // Q)
            dve.wait_ge(condition_loaded, 16 * PAIR)
            nc.vector.tensor_scalar(table_row[:, :], condition[:, :], float(K), piece[:, 0:1],
                                    ALU.mult, ALU.add).then_inc(rows_known, 1)
            dve.wait_ge(w_gathered, 16)
            nc.vector.transpose(w_all[:, :, :], gathered[:, :].rearrange("p (c d) -> p d c", d=D)
                                ).then_inc(w_transposed, 1)
            with dve.Fori(0, TURNS) as turn:
                for s in range(U):
                    dve.wait_ge(multiplied, turn * U + (s + 1))
                    xs = x_sb[:, bass.ds(turn * U + s, 1), :]
                    nc.vector.tensor_tensor(xs, product[s][:, :].unsqueeze(1), xs, ALU.add).then_inc(added, 1)


def kernel(x, itok_B_1_198, L0_cond_weights):
    import numpy as np
    import concourse.bacc as bacc
    from concourse.bass_utils import run_bass_kernel_spmd

    nc = bacc.Bacc("TRN2", target_bir_lowering=False, num_devices=1)
    arrays = {"x": np.ascontiguousarray(x),
              "conditions": np.ascontiguousarray(itok_B_1_198).reshape(-1, 1),
              "weights": np.ascontiguousarray(L0_cond_weights)}
    args = [nc.dram_tensor(name, a.shape, mybir.dt.from_np(a.dtype), kind="ExternalInput").ap()
            for name, a in arrays.items()]
    out = nc.dram_tensor("out", x.shape, mybir.dt.float32, kind="ExternalOutput").ap()
    conditioned_residual_kernel(nc, *args, out)
    result = run_bass_kernel_spmd(nc, [arrays], core_ids=[0])
    return result.results[0]["out"]
```
